# Optimizing a Trainium2 kernel written in Bass

```python
import numpy as np
import jax
import jax.numpy as jnp

def _softmax(x, axis=-1):
    return jax.nn.softmax(x, axis=axis)

def _gelu(x):
    return jax.nn.gelu(x, approximate=True)

def _silu(x):
    return jax.nn.silu(x)

def _sigmoid(x):
    return jax.nn.sigmoid(x)

def _layernorm(x, axis=-1, eps=1e-05):
    m = jnp.mean(x, axis=axis, keepdims=True)
    v = jnp.var(x, axis=axis, keepdims=True)
    return (x - m) / jnp.sqrt(v + eps)

def _scatter_add(tgt, idx, src, axis=0):
    return tgt.at[idx].add(src)

def _segment_sum(src, seg, n):
    return jax.ops.segment_sum(src, seg, n)
kernel_name = 'mk_gnn_preln_d1_gnn_r8_ed84ac'

def setup_inputs(seed: int=0):
    np.random.seed(seed)
    _w = jnp.asarray

    def _rec_inputs():
        import jax
        import jax.numpy as jnp
        _gk = jax.random.key(seed)
        x = -0.0005121 + 1.001 * jax.random.normal(jax.random.fold_in(_gk, 1), (12500, 64), jnp.float32)
        _s = jax.random.randint(jax.random.fold_in(_gk, 2), (200000,), 0, 12500, jnp.int32)
        _d = jax.random.randint(jax.random.fold_in(_gk, 3), (200000,), 0, 12500, jnp.int32)
        _loop = jnp.arange(12500, dtype=jnp.int32)
        src = jnp.concatenate([_s, _d, _loop])
        dst = jnp.concatenate([_d, _s, _loop])
        _o = jnp.argsort(dst, stable=True)
        src = src[_o]
        dst = dst[_o]
        edge_attr_32 = 0.000196303 + 1.00016 * jax.random.normal(jax.random.fold_in(_gk, 11), (412500, 32), jnp.float32)
        return (x, src, dst, edge_attr_32)
    x, src, dst, edge_attr_32 = _rec_inputs()

    def _L0_gnn_setup():
        import jax, jax.numpy as jnp
        import numpy as np
        N_NODES = 6250
        N_EDGES = 100000
        F_X = 64
        F_E = 32
        H = 128
        F_OUT = 64

        def scatter_mean(vals, idx, num_segments):
            s = jax.ops.segment_sum(vals, idx, num_segments=num_segments)
            cnt = jax.ops.segment_sum(jnp.ones((vals.shape[0],), dtype=vals.dtype), idx, num_segments=num_segments)
            return s / jnp.maximum(cnt, 1.0)[:, None]
        key = jax.random.key(seed)
        ks = jax.random.split(key, 12)
        x = jax.random.normal(ks[0], (N_NODES, F_X), dtype=jnp.float32)
        edge_index = jax.random.randint(ks[1], (2, N_EDGES), 0, N_NODES)
        edge_attr = jax.random.normal(ks[2], (N_EDGES, F_E), dtype=jnp.float32)

        def lin(k, fan_in, fan_out):
            kw, kb = jax.random.split(k)
            bound = 1.0 / np.sqrt(fan_in)
            W = jax.random.uniform(kw, (fan_in, fan_out), minval=-bound, maxval=bound, dtype=jnp.float32)
            b = jax.random.uniform(kb, (fan_out,), minval=-bound, maxval=bound, dtype=jnp.float32)
            return (W, b)
        W1, b1 = lin(ks[3], F_X + F_E, H)
        W2, b2 = lin(ks[4], H, F_OUT)
        W3, b3 = lin(ks[5], F_X + F_OUT, H)
        W4, b4 = lin(ks[6], H, F_OUT)
        return {'x': x, 'edge_index': edge_index, 'edge_attr': edge_attr, 'W1': W1, 'b1': b1, 'W2': W2, 'b2': b2, 'W3': W3, 'b3': b3, 'W4': W4, 'b4': b4}
    _L0_gnn_all = _L0_gnn_setup()
    _L0_gnn_in = {k: v for k, v in _L0_gnn_all.items() if k in ('W1', 'b1', 'W2', 'b2', 'W3', 'b3', 'W4', 'b4')}
    del _L0_gnn_all
    return {'x': x, 'src': src, 'dst': dst, 'edge_attr_32': edge_attr_32, 'L0_gnn_W1': _L0_gnn_in['W1'], 'L0_gnn_b1': _L0_gnn_in['b1'], 'L0_gnn_W2': _L0_gnn_in['W2'], 'L0_gnn_b2': _L0_gnn_in['b2'], 'L0_gnn_W3': _L0_gnn_in['W3'], 'L0_gnn_b3': _L0_gnn_in['b3'], 'L0_gnn_W4': _L0_gnn_in['W4'], 'L0_gnn_b4': _L0_gnn_in['b4']}

def reference(x, src, dst, edge_attr_32, L0_gnn_W1, L0_gnn_b1, L0_gnn_W2, L0_gnn_b2, L0_gnn_W3, L0_gnn_b3, L0_gnn_W4, L0_gnn_b4):
    import jax
    import jax.numpy as jnp

    def _L0_gnn_ref(x, edge_index, edge_attr, W1, b1, W2, b2, W3, b3, W4, b4):
        import jax, jax.numpy as jnp
        import numpy as np
        N_NODES = 6250
        N_EDGES = 100000
        F_X = 64
        F_E = 32
        H = 128
        F_OUT = 64

        def scatter_mean(vals, idx, num_segments):
            s = jax.ops.segment_sum(vals, idx, num_segments=num_segments)
            cnt = jax.ops.segment_sum(jnp.ones((vals.shape[0],), dtype=vals.dtype), idx, num_segments=num_segments)
            return s / jnp.maximum(cnt, 1.0)[:, None]
        row, col = (edge_index[0], edge_index[1])
        h = jnp.concatenate([x[row], edge_attr], axis=1)
        h = jax.nn.relu(h @ W1 + b1)
        h = h @ W2 + b2
        agg = scatter_mean(h, col, x.shape[0])
        g = jnp.concatenate([x, agg], axis=1)
        g = jax.nn.relu(g @ W3 + b3)
        return g @ W4 + b4
    edge_index = jnp.stack([src, dst])
    h = jnp.maximum(_layernorm(x, axis=-1), 0.0)
    x = x + _L0_gnn_ref(h, edge_index, edge_attr_32, L0_gnn_W1, L0_gnn_b1, L0_gnn_W2, L0_gnn_b2, L0_gnn_W3, L0_gnn_b3, L0_gnn_W4, L0_gnn_b4)
    return x

_drawn_inputs = setup_inputs


def setup_inputs(seed=0):
    import zlib

    import numpy as np

    out = dict(_drawn_inputs(seed))
    spreads = {}
    factors = {'edge_attr_32': 8.0,
     'L0_gnn_W1': 5.844,
     'L0_gnn_b1': 8.0,
     'L0_gnn_W2': 2.92,
     'L0_gnn_b2': 8.0,
     'L0_gnn_b3': 3.032}
    for name, (base, spread) in spreads.items():
        noise = np.random.default_rng([zlib.crc32(name.encode()), seed]).standard_normal(out[name].shape)
        drawn = base * np.exp(spread * noise) if base else spread * noise
        out[name] = jnp.asarray(drawn.astype(out[name].dtype))
    for name, factor in factors.items():
        out[name] = (out[name] * factor).astype(out[name].dtype)
    return out
```

```python
from contextlib import ExitStack

import concourse.bass as bass
from concourse import mybir

F32 = mybir.dt.float32
BF16 = mybir.dt.bfloat16
I32 = mybir.dt.int32
ALU = mybir.AluOpType
ACT = mybir.ActivationFunctionType
AX = mybir.AxisListType

P = 128
N_NODES, F_X, F_E, HID, F_OUT = 12500, 64, 32, 128, 64
N_EDGES = 412500
EPS = 1e-5

TPG = 4
GROUP = TPG * P
GROUPS = -(-N_EDGES // GROUP)
BODY = 13
TURNS = GROUPS // BODY
PARTS = ((0, 7), (7, BODY))
WINDOW = 64

NODE_TILES = -(-N_NODES // P)
PAIRS = NODE_TILES // 2
PAIR = 2 * P
NODES_PAD = NODE_TILES * P
CHUNKS = 7
CPAIRS = PAIRS // CHUNKS
CTILES = 2 * CPAIRS
CCOLS = CTILES * F_X

LAG = 15
EARLY_PAIRS = TURNS - LAG

assert GROUPS == TURNS * BODY and NODE_TILES == 2 * PAIRS and PAIRS == CHUNKS * CPAIRS
assert CHUNKS % 2 == 1


def gnn_layer(nc, x_t, src_t, dst_t, edge_t, w1, b1, w2, b2, w3, b3, w4, b4, y_t):
    proj = nc.dram_tensor("projected_nodes", [NODES_PAD, HID], F32, kind="Internal").ap()
    proj_tiles = proj.rearrange("(i p) h -> p i h", p=P)

    ctx = ExitStack()
    with ctx:
        def sb(name, shape, dt=F32):
            return ctx.enter_context(nc.sbuf_tensor(name, shape, dt))

        def pb(name, shape):
            return ctx.enter_context(nc.psum_tensor(name, shape, F32))

        def sem(name):
            return ctx.enter_context(nc.semaphore(name))

        agg = sb("agg", [P, 2, NODES_PAD + WINDOW])
        hT = sb("hT", [P, PAIRS, P])
        dst_rel = sb("dst_rel", [P, GROUPS * TPG])
        dst_int = dst_rel[:, :].bitcast(I32)
        base_i = sb("base_i", [1, GROUPS], I32)
        base_f = sb("base_f", [1, GROUPS])
        limit = sb("limit", [1, GROUPS])
        gat = sb("gat", [P, BODY, GROUP])
        edg = sb("edg", [P, BODY, P])
        idx = sb("idx", [P, BODY * TPG], I32)
        sel = sb("sel", [P, 2, TPG, WINDOW])
        xin = sb("xin", [P, 2, CCOLS])
        sq = sb("sq", [P, CCOLS])
        lnsum = sb("lnsum", [P, CTILES])
        lnvar = sb("lnvar", [P, CTILES])
        lnstd = sb("lnstd", [P, CTILES])
        lnrstd = sb("lnrstd", [P, CTILES])
        w1x = sb("w1x", [P, 2 * HID])
        w1e = sb("w1e", [P, TPG, HID])
        w2s = sb("w2s", [P, F_OUT])
        b2row = sb("b2row", [P, F_OUT])
        w3x = sb("w3x", [P, 2, HID])
        w3a = sb("w3a", [F_OUT, HID])
        w4s = sb("w4s", [P, F_OUT])
        b1b = sb("b1b", [P, HID])
        b4b = sb("b4b", [P, F_OUT])
        b3c = sb("b3c", [P, 1])
        epsc = sb("epsc", [P, 1])
        windc = sb("windc", [P, 1])
        ident = sb("ident", [P, P])
        onesf = sb("onesf", [P, P])
        onesb = sb("onesb", [P, P], BF16)
        iotaf = sb("iotaf", [P, WINDOW])
        viol = sb("viol", [P, 3])
        vsum = sb("vsum", [1, 1])
        flag = sb("flag", [1, 1], I32)
        rcnt = sb("rcnt", [F_OUT, PAIR])
        mean = sb("mean", [F_OUT, PAIR])
        gact = sb("gact", [P, PAIR])
        xpair = sb("xpair", [P, 2 * F_X])
        ypair = sb("ypair", [P, 2 * F_OUT])

        slots = gat[:, :, :].rearrange("p s n -> p (s n)")
        pout = slots[:, 0:2 * CTILES * HID].rearrange("p (b i h) -> p b i h", b=2, h=HID)
        trash = slots[:, 2 * CTILES * HID:2 * CTILES * HID + GROUPS * TPG // 2].bitcast(BF16)
        gen_iota = slots[:, 1 * GROUP:1 * GROUP + PAIR]
        gen_sel = slots[:, 2 * GROUP:4 * GROUP].rearrange("p (j w) -> p j w", j=TPG)
        gen_dst = slots[:, 4 * GROUP:4 * GROUP + TPG]
        gen_dst_i = slots[:, 5 * GROUP:5 * GROUP + TPG].bitcast(I32)

        mps = pb("mps", [P, 2, GROUP])
        wps = pb("wps", [P, 2, 512])
        ips = pb("ips", [P, 512])
        nps = pb("nps", [P, 3, 512])
        iota_ps = ips[:, 0:WINDOW]
        s2_ps = nps[0:F_OUT, 0, 0:PAIR]
        g_ps = nps[:, 1, 0:PAIR]
        o_ps = nps[:, 2, 0:2 * F_OUT]
        tps = mps[:, :, :].rearrange("p b (q n) -> p b q n", q=4)
        ups = wps
        base_ps = nps[:, 0:2, 0:GROUPS // 2]
        viol_ps = nps[0:1, 2, 0:3]
        gen_ps = wps[:, 0, :].rearrange("p (c n) -> p c n", c=2)

        weights_in = sem("weights_in")
        bias_in = sem("bias_in")
        dst_in = sem("dst_in")
        pad_zeroed = sem("pad_zeroed")
        pool_consts = sem("pool_consts")
        dve_consts = sem("dve_consts")
        iota_up = sem("iota_up")
        base_copied = sem("base_copied")
        base_spread = sem("base_spread")
        rel_ready = sem("rel_ready")
        limit_ready = sem("limit_ready")
        low_checked = sem("low_checked")
        all_checked = sem("all_checked")
        viol_summed = sem("viol_summed")
        vsum_ready = sem("vsum_ready")
        flag_ready = sem("flag_ready")
        x_in = [sem(f"x_in{b}") for b in range(2)]
        ln_sum = sem("ln_sum")
        ln_centred = sem("ln_centred")
        ln_squared = sem("ln_squared")
        ln_var = sem("ln_var")
        ln_std = sem("ln_std")
        ln_rstd = sem("ln_rstd")
        ln_scaled = sem("ln_scaled")
        h_turned = sem("h_turned")
        h_kept = sem("h_kept")
        projected = sem("projected")
        biased = sem("biased")
        proj_out = [sem(f"proj_out{b}") for b in range(2)]
        agg_zeroed = sem("agg_zeroed")
        settled = sem("settled")
        idx_in = [sem(f"idx_in{h}") for h in range(2)]
        edg_in = [sem(f"edg_in{h}") for h in range(2)]
        gathered = [sem(f"gathered{s}") for s in range(BODY)]
        edge_mm = sem("edge_mm")
        summed = sem("summed")
        relued = sem("relued")
        selected = sem("selected")
        window_mm = sem("window_mm")
        accumulated = sem("accumulated")
        xpair_in = sem("xpair_in")
        cnt_clamped = sem("cnt_clamped")
        cnt_inverted = sem("cnt_inverted")
        w2_mm = sem("w2_mm")
        averaged = sem("averaged")
        w3_mm = sem("w3_mm")
        g_relued = sem("g_relued")
        w4_mm = sem("w4_mm")
        y_biased = sem("y_biased")
        y_ready = sem("y_ready")
        y_out = sem("y_out")
        gen_in = sem("gen_in")
        gen_gathered = sem("gen_gathered")
        gen_edge_mm = sem("gen_edge_mm")
        gen_dst_f = sem("gen_dst_f")
        gen_summed = sem("gen_summed")
        gen_relued = sem("gen_relued")
        gen_iota_up = sem("gen_iota_up")
        gen_selected = sem("gen_selected")
        gen_stepped = sem("gen_stepped")
        gen_mm = sem("gen_mm")
        gen_acc = sem("gen_acc")

        def done(i, s):
            return i * BODY + (BODY + s + 1)

        def user_before(s, bufs):
            if s >= bufs:
                return s - bufs
            return max(q for q in range(BODY) if q % bufs == s % bufs) - BODY

        def settle(eng):
            eng.sem_inc(settled, 1)

        def path(eng, fast, general):
            eng.wait_ge(flag_ready, 1)
            taken = eng.value_load(flag[0:1, 0:1])
            with eng.If(taken == 0):
                fast()
            with eng.Else():
                general()

        block = ctx.enter_context(nc.Block())

        @block.sync
        def _(sp):
            def load_x(c, b):
                sp.dma_start(xin[:, b, :], x_t[:, bass.ds(c * CCOLS, CCOLS)]).then_inc(x_in[b], 16)

            def store_proj(c, b, pieces_before):
                sp.wait_ge(biased, pieces_before + 4)
                sp.dma_start(proj_tiles[:, bass.ds(c * CTILES, CTILES), :], pout[:, b, :, :])\
                  .then_inc(proj_out[b], 16)

            def load_part(i, h):
                lo, hi = PARTS[h]
                sp.dma_start(idx[:, lo * TPG:hi * TPG],
                             src_t[:, bass.ds(i * (BODY * TPG) + lo * TPG, (hi - lo) * TPG)])\
                  .then_inc(idx_in[h], 16)
                sp.dma_start(edg[:, lo:hi, :].rearrange("p g e -> p (g e)"),
                             edge_t[:, bass.ds(i * (BODY * P) + lo * P, (hi - lo) * P)])\
                  .then_inc(edg_in[h], 16)

            def node_load(c):
                sp.dma_start(xpair[:, :], x_t[:, bass.ds(c * (2 * F_X), 2 * F_X)]).then_inc(xpair_in, 16)

            def node_store(c):
                sp.wait_ge(y_ready, c + 1)
                sp.dma_start(y_t[:, bass.ds(c * (2 * F_OUT), 2 * F_OUT)], ypair[:, :]).then_inc(y_out, 16)
                sp.wait_ge(y_out, c * 16 + 16)
                settle(sp)

            load_x(0, 0)
            sp.dma_start(dst_int, dst_t).then_inc(dst_in, 16)
            load_x(1, 1)
            sp.dma_start(w2s[:, :], w2).then_inc(weights_in, 16)
            sp.dma_start(w3a[:, :], w3[F_X:F_X + F_OUT, :]).then_inc(weights_in, 16)
            sp.dma_start(w4s[:, :], w4).then_inc(weights_in, 16)
            sp.dma_start(b3c[:, :], b3.rearrange("(h a) -> h a", a=1)).then_inc(weights_in, 16)
            sp.wait_ge(pad_zeroed, 1)
            for j in range(TPG):
                sp.dma_start(w1e[j * F_E:(j + 1) * F_E, j, :], w1[F_X:F_X + F_E, :]).then_inc(weights_in, 16)
            sp.dma_start(b4b[:, :], b4.partition_broadcast(P)).then_inc(weights_in, 16)

            def next_chunk(c, b, load=True):
                sp.wait_ge(h_turned, c * 2 + 2)
                if load:
                    load_x(c + 2, b)
                store_proj(c, b, c * 4)

            with sp.Fori(0, (CHUNKS - 3) // 2) as j:
                next_chunk(j * 2, 0)
                next_chunk(j * 2 + 1, 1)
            next_chunk(CHUNKS - 3, 0)
            next_chunk(CHUNKS - 2, 1, load=False)
            store_proj(CHUNKS - 1, 0, (CHUNKS - 1) * 4)
            sp.wait_ge(proj_out[0], 16 * ((CHUNKS + 1) // 2))
            sp.wait_ge(proj_out[1], 16 * (CHUNKS // 2))

            def fast():
                load_part(0, 0)
                load_part(0, 1)

                def turn(i, pair):
                    for h, (lo, hi) in enumerate(PARTS):
                        if pair is not None and h == 1:
                            node_store(pair)
                        for s in range(lo, hi):
                            sp.wait_ge(gathered[s], i * (16 * TPG) + 16 * TPG)
                        settle(sp)
                        sp.wait_ge(edge_mm, done(i, hi - 1))
                        load_part(i + 1, h)
                        if pair is not None and h == 0:
                            node_load(pair)

                with sp.Fori(0, LAG) as i:
                    turn(i, None)
                with sp.Fori(0, EARLY_PAIRS - 1) as c:
                    turn(c + LAG, c)
                for c in range(EARLY_PAIRS - 1, PAIRS):
                    node_load(c)
                    node_store(c)

            def general():
                with sp.Fori(0, GROUPS) as k:
                    sp.wait_ge(gen_acc, (k + 1) * PAIRS)
                    sp.dma_start(idx[:, 0:TPG], src_t[:, bass.ds(k * TPG, TPG)]).then_inc(gen_in, 16)
                    sp.dma_start(gen_dst_i, dst_t[:, bass.ds(k * TPG, TPG)]).then_inc(gen_in, 16)
                    sp.dma_start(edg[:, 0, :], edge_t[:, bass.ds(k * P, P)]).then_inc(gen_in, 16)
                with sp.Fori(0, PAIRS) as c:
                    node_load(c)
                    node_store(c)

            path(sp, fast, general)

        @block.gpsimd
        def _(pool):
            piece = agg[:, :, :].rearrange("p c n -> p (c n)")
            zeros = 2 * (NODES_PAD + WINDOW) // (CHUNKS + 1)
            assert zeros * (CHUNKS + 1) == 2 * (NODES_PAD + WINDOW)

            pool.memset(w1e[:, :, :], 0.0).then_inc(pad_zeroed, 1)
            pool.memset(w1x[:, :], 0.0).then_inc(pad_zeroed, 1)
            pool.memset(w3x[:, :, :], 0.0).then_inc(pad_zeroed, 1)
            pool.memset(b2row[:, :], 0.0).then_inc(pad_zeroed, 1)
            pool.memset(ident[:, :], 0.0).then_inc(pool_consts, 1)
            pool.iota(iotaf[:, :], [[1, WINDOW]], base=0, channel_multiplier=0,
                      allow_small_or_imprecise_dtypes=True).then_inc(pool_consts, 1)
            pool.iota(limit[:, :], [[PAIR, TURNS], [0, BODY]], base=-PAIR * (LAG - 1), channel_multiplier=0,
                      allow_small_or_imprecise_dtypes=True).then_inc(pool_consts, 1)
            pool.wait_ge(pool_consts, 3)
            pool.affine_select(out=ident[:, :], in_=ident[:, :], compare_op=ALU.not_equal, fill=1.0, base=0,
                               pattern=[[-1, P]], channel_multiplier=1).then_inc(pool_consts, 1)
            pool.memset(piece[:, 0:zeros], 0.0).then_inc(agg_zeroed, 1)

            def scale(c, b):
                pool.wait_ge(ln_rstd, c + 1)
                v = xin[:, b, :].rearrange("p (i f) -> p i f", f=F_X)
                pool.tensor_tensor(v, v, lnrstd[:, :].unsqueeze(2).to_broadcast([P, CTILES, F_X]), ALU.mult)\
                    .then_inc(ln_scaled, 1)
                pool.memset(piece[:, bass.ds((c + 1) * zeros, zeros)], 0.0).then_inc(agg_zeroed, 1)

            for c in range(CHUNKS):
                scale(c, c % 2)

            pool.wait_ge(proj_out[0], 16 * ((CHUNKS + 1) // 2))
            pool.wait_ge(proj_out[1], 16 * (CHUNKS // 2))

            def gather(s, j, signal):
                pool.indirect_dma_start(
                    out=gat[:, s, j * P:(j + 1) * P], out_offset=None, in_=proj[:, :],
                    in_offset=bass.IndirectOffsetOnAxis(ap=idx[:, s * TPG + j:s * TPG + j + 1], axis=0))\
                    .then_inc(signal, 16)

            def fast():
                with pool.Fori(0, TURNS) as i:
                    for s in range(BODY):
                        for h, (lo, hi) in enumerate(PARTS):
                            if s == lo:
                                pool.wait_ge(idx_in[h], i * 16 + 16)
                        pool.wait_ge(window_mm, done(i, s - BODY))
                        settle(pool)
                        for j in range(TPG):
                            gather(s, j, gathered[s])

            def general():
                pool.iota(gen_iota, [[1, PAIR]], base=0, channel_multiplier=0,
                          allow_small_or_imprecise_dtypes=True).then_inc(gen_iota_up, 1)
                with pool.Fori(0, GROUPS) as k:
                    pool.wait_ge(gen_in, k * 48 + 48)
                    settle(pool)
                    for j in range(TPG):
                        gather(0, j, gen_gathered)

            path(pool, fast, general)

        @block.scalar
        def _(act):
            def square(c, b):
                act.wait_ge(ln_centred, c + 1)
                nc.scalar.activation(sq[:, :], xin[:, b, :], ACT.Square).then_inc(ln_squared, 1)

            def std(c):
                act.wait_ge(ln_var, c + 1)
                nc.scalar.activation(lnstd[:, :], lnvar[:, :], ACT.Sqrt, bias=epsc[:, :], scale=1.0 / F_X)\
                  .then_inc(ln_std, 1)

            def keep(c):
                for t, (lo, hi) in enumerate(((0, 4), (4, CPAIRS))):
                    act.wait_ge(h_turned, c * 2 + t + 1)
                    nc.scalar.activation(hT[:, bass.ds(c * CPAIRS + lo, hi - lo), :], tps[:, t, 0:hi - lo, :],
                                         ACT.Relu).then_inc(h_kept, 1)

            act.wait_ge(pad_zeroed, 4)
            for q in range(2):
                act.dma_start(w1x[q * F_X:(q + 1) * F_X, q * HID:(q + 1) * HID], w1[0:F_X, :])\
                   .then_inc(bias_in, 16)
            act.dma_start(b1b[:, :], b1.partition_broadcast(P)).then_inc(bias_in, 16)
            for q in range(2):
                act.dma_start(w3x[q * F_X:(q + 1) * F_X, q, :], w3[0:F_X, :]).then_inc(weights_in, 16)
            act.dma_start(b2row[0:1, :], b2.rearrange("(a n) -> a n", a=1)).then_inc(weights_in, 16)

            act.wait_ge(dve_consts, 3)
            square(0, 0)
            std(0)
            act.wait_ge(rel_ready, 2)
            nc.scalar.activation(trash, dst_rel[:, :], ACT.Relu, scale=-1.0, accum_out=viol[:, 0:1])\
              .then_inc(low_checked, 1)
            act.wait_ge(low_checked, 1)
            nc.scalar.activation(trash, dst_rel[:, :], ACT.Relu, bias=windc[:, :], accum_out=viol[:, 1:2])\
              .then_inc(all_checked, 1)
            act.wait_ge(limit_ready, 1)
            nc.scalar.activation(base_f[:, :], limit[:, :], ACT.Relu, accum_out=viol[0:1, 2:3])\
              .then_inc(all_checked, 1)
            square(1, 1)
            keep(0)
            std(1)
            with act.Fori(0, (CHUNKS - 1) // 2 - 1) as j:
                for b in range(2):
                    c = j * 2 + b
                    square(c + 2, b)
                    keep(c + 1)
                    std(c + 2)
            square(CHUNKS - 1, 0)
            keep(CHUNKS - 2)
            std(CHUNKS - 1)
            keep(CHUNKS - 1)

            def node_relu(c):
                act.wait_ge(w3_mm, c + 1)
                nc.scalar.activation(gact[:, :], g_ps, ACT.Relu, bias=b3c[:, :]).then_inc(g_relued, 1)

            act.wait_ge(weights_in, 16 * 12)

            def fast():
                def turn(i, pair):
                    for s in range(BODY):
                        act.wait_ge(summed, done(i, s))
                        nc.scalar.activation(gat[:, s, :], gat[:, s, :], ACT.Relu).then_inc(relued, 1)
                        if pair is not None and s == 5:
                            node_relu(pair)

                with act.Fori(0, LAG) as i:
                    turn(i, None)
                with act.Fori(0, EARLY_PAIRS) as c:
                    turn(c + LAG, c)
                for c in range(EARLY_PAIRS, PAIRS):
                    node_relu(c)

            def general():
                with act.Fori(0, GROUPS) as k:
                    act.wait_ge(gen_summed, k + 1)
                    nc.scalar.activation(gat[:, 0, :], gat[:, 0, :], ACT.Relu).then_inc(gen_relued, 1)
                with act.Fori(0, PAIRS) as c:
                    node_relu(c)

            path(act, fast, general)

        @block.tensor
        def _(pe):
            pe.wait_ge(dve_consts, 3)
            pe.wait_ge(base_copied, 2)
            for h in range(2):
                mm = nc.tensor.matmul(base_ps[:, h, :], onesf[0:1, :],
                                      base_f[0:1, h * (GROUPS // 2):(h + 1) * (GROUPS // 2)],
                                      start=True, stop=True)
            mm.then_inc(base_spread, 1)
            pe.wait_ge(pool_consts, 4)
            pe.wait_ge(bias_in, 48)

            def project(c, b, first=False):
                pe.wait_ge(ln_scaled, c + 1)
                for t, (lo, hi) in enumerate(((0, 4), (4, CPAIRS))):
                    if not first:
                        pe.wait_ge(h_kept, c * 2 + (t - 1))
                    for q in range(lo, hi):
                        mm = nc.tensor.transpose(tps[:, t, q - lo, :], xin[:, b, q * P:(q + 1) * P], ident[:, :])
                    mm.then_inc(h_turned, 1)
                for u in range(4):
                    pe.wait_ge(h_kept, c * 2 + (1 if u < 2 else 2))
                    if not (first and u < 2):
                        pe.wait_ge(biased, c * 4 + (u - 1))
                    for q in range(2 * u, min(2 * u + 2, CPAIRS)):
                        mm = nc.tensor.matmul(ups[:, u % 2, (q % 2) * PAIR:(q % 2 + 1) * PAIR],
                                              hT[:, c * CPAIRS + q, :], w1x[:, :], start=True, stop=True)
                    mm.then_inc(projected, 1)

            project(0, 0, first=True)
            for c in range(1, CHUNKS):
                project(c, c % 2)

            pe.wait_ge(all_checked, 2)
            nc.tensor.matmul(viol_ps, onesf[:, 0:1], viol[:, :], start=True, stop=True).then_inc(viol_summed, 1)
            pe.wait_ge(weights_in, 16 * 12)
            pe.wait_ge(agg_zeroed, CHUNKS + 1)
            pe.wait_ge(biased, 4 * CHUNKS)

            def edge_products(buf, s):
                return nc.tensor.matmul(mps[:, buf, :], edg[:, s, :], w1e[:, :, :].rearrange("p j h -> p (j h)"),
                                        start=True, stop=True)

            def node_w2(c):
                cols = bass.ds(c * PAIR, PAIR)
                nc.tensor.matmul(s2_ps, w2s[:, :], agg[:, 0, cols], start=True, stop=False)
                nc.tensor.matmul(s2_ps, b2row[:, :], agg[:, 1, cols], start=False, stop=True).then_inc(w2_mm, 1)

            def node_w3(c):
                pe.wait_ge(averaged, c + 1)
                nc.tensor.matmul(g_ps, w3a[:, :], mean[:, :], start=True, stop=False)
                for q in range(2):
                    mm = nc.tensor.matmul(g_ps[:, q * P:(q + 1) * P], w3x[:, q, :],
                                          hT[:, bass.ds(c, 1), :].rearrange("p a n -> p (a n)"),
                                          start=False, stop=(q == 1))
                mm.then_inc(w3_mm, 1)

            def node_w4(c):
                pe.wait_ge(g_relued, c + 1)
                for q in range(2):
                    mm = nc.tensor.matmul(o_ps[:, q * F_OUT:(q + 1) * F_OUT], gact[:, q * P:(q + 1) * P],
                                          w4s[:, :], start=True, stop=True)
                mm.then_inc(w4_mm, 1)

            def fast():
                def window_sums(i, s):
                    pe.wait_ge(relued, done(i, s))
                    pe.wait_ge(selected, done(i, s))
                    pe.wait_ge(accumulated, done(i, user_before(s, 2)))
                    for j in range(TPG):
                        nc.tensor.matmul(wps[:, s % 2, 0:WINDOW], gat[:, s, j * P:(j + 1) * P], sel[:, s % 2, j, :],
                                         start=(j == 0), stop=(j == TPG - 1))
                    for j in range(TPG):
                        mm = nc.tensor.matmul(wps[:, s % 2, WINDOW:2 * WINDOW], onesb[:, :],
                                              sel[:, s % 2, j, :].bitcast(BF16)[:, 1::2],
                                              start=(j == 0), stop=(j == TPG - 1))
                    mm.then_inc(window_mm, 1)

                def turn(i, pair):
                    for s in range(BODY):
                        for h, (lo, hi) in enumerate(PARTS):
                            if s == lo:
                                pe.wait_ge(edg_in[h], i * 16 + 16)
                        pe.wait_ge(summed, done(i, user_before(s, 2)))
                        edge_products(s % 2, s).then_inc(edge_mm, 1)
                        if s >= 1:
                            window_sums(i, s - 1)
                        if pair is not None and s == 2:
                            pe.wait_ge(accumulated, done(i, -1))
                            node_w2(pair)
                        if pair is not None and s == 4:
                            node_w3(pair)
                        if pair is not None and s == 6:
                            node_w4(pair)
                    window_sums(i, BODY - 1)

                with pe.Fori(0, LAG) as i:
                    turn(i, None)
                with pe.Fori(0, EARLY_PAIRS) as c:
                    turn(c + LAG, c)
                pe.wait_ge(accumulated, done(TURNS, -1))
                for c in range(EARLY_PAIRS, PAIRS):
                    node_w2(c)
                    node_w3(c)
                    node_w4(c)

            def general():
                with pe.Fori(0, GROUPS) as k:
                    pe.wait_ge(gen_in, k * 48 + 48)
                    edge_products(0, 0).then_inc(gen_edge_mm, 1)
                    pe.wait_ge(gen_relued, k + 1)
                    settle(pe)
                    with pe.Fori(0, PAIRS) as b:
                        pe.wait_ge(gen_selected, k * PAIRS + b + 1)
                        for j in range(TPG):
                            nc.tensor.matmul(gen_ps[:, 0, :], gat[:, 0, j * P:(j + 1) * P], gen_sel[:, j, :],
                                             start=(j == 0), stop=(j == TPG - 1))
                        for j in range(TPG):
                            mm = nc.tensor.matmul(gen_ps[:, 1, :], onesb[:, :],
                                                  gen_sel[:, j, :].bitcast(BF16)[:, 1::2],
                                                  start=(j == 0), stop=(j == TPG - 1))
                        mm.then_inc(gen_mm, 1)
                pe.wait_ge(gen_acc, (GROUPS + 1) * PAIRS)
                with pe.Fori(0, PAIRS) as c:
                    node_w2(c)
                    node_w3(c)
                    node_w4(c)

            path(pe, fast, general)

        @block.vector
        def _(dve):
            for group_sem in (edge_mm, summed, relued, selected, window_mm, accumulated):
                dve.sem_inc(group_sem, BODY)
            dve.sem_inc(gen_acc, PAIRS)
            nc.vector.memset(onesf[:, :], 1.0).then_inc(dve_consts, 1)
            nc.vector.memset(epsc[:, :], EPS).then_inc(dve_consts, 1)
            nc.vector.memset(windc[:, :], -float(WINDOW - 1)).then_inc(dve_consts, 1)
            nc.vector.memset(onesb[:, :], 1.0)
            nc.vector.memset(viol[:, :], 0.0).then_inc(dve_consts, 1)

            dve.wait_ge(dst_in, 16)
            first_dst = dst_int[0:1, 0:GROUPS * TPG:TPG]
            nc.vector.tensor_copy(base_i[:, :], first_dst).then_inc(base_copied, 1)
            nc.vector.tensor_copy(base_f[:, :], first_dst).then_inc(base_copied, 1)
            dve.wait_ge(pool_consts, 3)
            nc.vector.tensor_copy(iota_ps, iotaf[:, :]).then_inc(iota_up, 1)

            def centre(c, b, occ):
                v = xin[:, b, :].rearrange("p (i f) -> p i f", f=F_X)
                dve.wait_ge(x_in[b], occ * 16 + 16)
                nc.vector.tensor_reduce(lnsum[:, :], v, AX.X, ALU.add).then_inc(ln_sum, 1)
                dve.wait_ge(ln_sum, c + 1)
                nc.vector.scalar_tensor_tensor(out=v, in0=lnsum[:, :].unsqueeze(2).to_broadcast([P, CTILES, F_X]),
                                               scalar=-1.0 / F_X, in1=v, op0=ALU.mult, op1=ALU.add)\
                  .then_inc(ln_centred, 1)

            def variance(c):
                dve.wait_ge(ln_squared, c + 1)
                nc.vector.tensor_reduce(lnvar[:, :], sq[:, :].rearrange("p (i f) -> p i f", f=F_X), AX.X, ALU.add)\
                  .then_inc(ln_var, 1)

            def inverse(c, first=False):
                dve.wait_ge(ln_std, c + 1)
                if not first:
                    dve.wait_ge(ln_scaled, c)
                nc.vector.reciprocal(lnrstd[:, :], lnstd[:, :]).then_inc(ln_rstd, 1)

            def bias(c, b, pieces):
                for u in pieces:
                    n = min(2, CPAIRS - 2 * u)
                    dve.wait_ge(projected, c * 4 + (u + 1))
                    nc.vector.tensor_tensor(
                        pout[:, b, 4 * u:4 * u + 2 * n, :],
                        ups[:, u % 2, 0:n * PAIR].rearrange("p (i h) -> p i h", h=HID),
                        b1b[:, :].unsqueeze(1).to_broadcast([P, 2 * n, HID]), ALU.add).then_inc(biased, 1)

            centre(0, 0, 0)
            dve.wait_ge(base_spread, 1)
            for h in range(2):
                half = slice(h * GROUPS * TPG // 2, (h + 1) * GROUPS * TPG // 2)
                nc.vector.tensor_tensor(
                    dst_rel[:, half].rearrange("p (g j) -> p g j", j=TPG),
                    dst_int[:, half].rearrange("p (g j) -> p g j", j=TPG),
                    base_ps[:, h, :].unsqueeze(2).to_broadcast([P, GROUPS // 2, TPG]), ALU.subtract)\
                  .then_inc(rel_ready, 1)
            dve.wait_ge(base_copied, 2)
            nc.vector.tensor_tensor(limit[:, :], limit[:, :], base_f[:, :], ALU.subtract).then_inc(limit_ready, 1)
            variance(0)
            inverse(0, first=True)
            dve.wait_ge(bias_in, 48)

            def step(c, b, occ, reuse):
                centre(c + 1, 1 - b, occ)
                if reuse is not None:
                    dve.wait_ge(proj_out[b], reuse)
                bias(c, b, (0, 1))
                variance(c + 1)
                bias(c, b, (2, 3))
                inverse(c + 1)

            dve.wait_ge(all_checked, 1)
            step(0, 0, 0, None)
            step(1, 1, 1, None)
            with dve.Fori(1, (CHUNKS - 1) // 2) as j:
                step(j * 2, 0, j, j * 16)
                step(j * 2 + 1, 1, j + 1, j * 16)
            dve.wait_ge(proj_out[0], 16 * (CHUNKS // 2))
            bias(CHUNKS - 1, 0, (0, 1, 2, 3))

            dve.wait_ge(viol_summed, 1)
            nc.vector.tensor_reduce(vsum[:, :], viol_ps, AX.X, ALU.add).then_inc(vsum_ready, 1)
            dve.wait_ge(vsum_ready, 1)
            nc.vector.tensor_scalar(flag[:, :], vsum[:, :], 1.0, None, ALU.min).then_inc(flag_ready, 1)
            dve.wait_ge(agg_zeroed, CHUNKS + 1)
            dve.wait_ge(iota_up, 1)

            def node_counts(c):
                nc.vector.tensor_scalar(rcnt[:, :], agg[0:F_OUT, 1, bass.ds(c * PAIR, PAIR)], 1.0, None, ALU.max)\
                  .then_inc(cnt_clamped, 1)
                dve.wait_ge(cnt_clamped, c + 1)
                nc.vector.reciprocal(rcnt[:, :], rcnt[:, :]).then_inc(cnt_inverted, 1)

            def node_mean(c):
                dve.wait_ge(w2_mm, c + 1)
                dve.wait_ge(cnt_inverted, c + 1)
                nc.vector.tensor_tensor(mean[:, :], s2_ps, rcnt[:, :], ALU.mult).then_inc(averaged, 1)

            def node_result(c):
                dve.wait_ge(w4_mm, c + 1)
                dve.wait_ge(xpair_in, c * 16 + 16)
                nc.vector.tensor_tensor(ypair[:, :].rearrange("p (i f) -> p i f", f=F_OUT),
                                        o_ps.rearrange("p (i f) -> p i f", f=F_OUT),
                                        b4b[:, :].unsqueeze(1).to_broadcast([P, 2, F_OUT]), ALU.add)\
                  .then_inc(y_biased, 1)
                dve.wait_ge(y_biased, c + 1)
                nc.vector.tensor_tensor(ypair[:, :], ypair[:, :], xpair[:, :], ALU.add).then_inc(y_ready, 1)

            def fast():
                def select(i, s):
                    dve.wait_ge(window_mm, done(i, user_before(s, 2)))
                    rel = dst_rel[:, bass.ds(i * (BODY * TPG) + s * TPG, TPG)]
                    nc.vector.tensor_tensor(sel[:, s % 2, :, :],
                                            iota_ps.unsqueeze(1).to_broadcast([P, TPG, WINDOW]),
                                            rel.unsqueeze(2).to_broadcast([P, TPG, WINDOW]), ALU.is_equal)\
                      .then_inc(selected, 1)

                def add_sources(i, s):
                    dve.wait_ge(edge_mm, done(i, s))
                    dve.wait_ge(gathered[s], i * (16 * TPG) + 16 * TPG)
                    nc.vector.tensor_tensor(gat[:, s, :], mps[:, s % 2, :], gat[:, s, :], ALU.add).then_inc(summed, 1)

                def accumulate(i, s):
                    base = dve.value_load(base_i[0:1, bass.ds(i * BODY + s, 1)], min_val=0, max_val=NODES_PAD)
                    dve.wait_ge(window_mm, done(i, s))
                    dve.wait_ge(accumulated, done(i, s - 1))
                    window = agg[:, :, bass.ds(base, WINDOW)]
                    nc.vector.tensor_tensor(window,
                                            wps[:, s % 2, 0:2 * WINDOW].rearrange("p (c w) -> p c w", c=2),
                                            window, ALU.add).then_inc(accumulated, 1)

                def turn(i, pair):
                    for s in range(BODY):
                        select(i, s)
                        add_sources(i, s)
                        if s >= 1:
                            accumulate(i, s - 1)
                        if pair is not None and s == 1:
                            node_counts(pair)
                        if pair is not None and s == 3:
                            node_mean(pair)
                        if pair is not None and s == 7:
                            node_result(pair)
                    accumulate(i, BODY - 1)

                with dve.Fori(0, LAG) as i:
                    turn(i, None)
                with dve.Fori(0, EARLY_PAIRS) as c:
                    turn(c + LAG, c)
                dve.wait_ge(accumulated, done(TURNS, -1))
                for c in range(EARLY_PAIRS, PAIRS):
                    node_counts(c)
                    node_mean(c)
                    node_result(c)

            def general():
                dve.wait_ge(gen_iota_up, 1)
                with dve.Fori(0, GROUPS) as k:
                    dve.wait_ge(gen_in, k * 48 + 48)
                    nc.vector.tensor_copy(gen_dst, gen_dst_i).then_inc(gen_dst_f, 1)
                    dve.wait_ge(gen_edge_mm, k + 1)
                    dve.wait_ge(gen_gathered, k * (16 * TPG) + 16 * TPG)
                    nc.vector.tensor_tensor(gat[:, 0, :], mps[:, 0, :], gat[:, 0, :], ALU.add).then_inc(gen_summed, 1)
                    dve.wait_ge(gen_dst_f, k + 1)
                    settle(dve)
                    with dve.Fori(0, PAIRS) as b:
                        dve.wait_ge(gen_acc, k * PAIRS + b + PAIRS)
                        nc.vector.tensor_tensor(gen_sel, gen_iota.unsqueeze(1).to_broadcast([P, TPG, PAIR]),
                                                gen_dst.unsqueeze(2).to_broadcast([P, TPG, PAIR]), ALU.is_equal)\
                          .then_inc(gen_selected, 1)
                        nc.vector.tensor_scalar(gen_dst, gen_dst, -float(PAIR), None, ALU.add).then_inc(gen_stepped, 1)
                        dve.wait_ge(gen_stepped, k * PAIRS + b + 1)
                        dve.wait_ge(gen_mm, k * PAIRS + b + 1)
                        pair_sums = agg[:, :, bass.ds(b * PAIR, PAIR)]
                        nc.vector.tensor_tensor(pair_sums, gen_ps, pair_sums, ALU.add).then_inc(gen_acc, 1)
                dve.wait_ge(gen_acc, (GROUPS + 1) * PAIRS)
                with dve.Fori(0, PAIRS) as c:
                    node_counts(c)
                    node_mean(c)
                    node_result(c)

            path(dve, fast, general)


def kernel(x, src, dst, edge_attr_32, L0_gnn_W1, L0_gnn_b1, L0_gnn_W2, L0_gnn_b2, L0_gnn_W3, L0_gnn_b3,
           L0_gnn_W4, L0_gnn_b4):
    import numpy as np
    import concourse.bacc as bacc
    from concourse.bass_utils import run_bass_kernel_spmd

    x_pad = np.zeros((NODES_PAD, F_X), np.float32)
    x_pad[:N_NODES] = np.asarray(x)
    src_pad = np.zeros(GROUPS * GROUP, np.int32)
    src_pad[:N_EDGES] = np.asarray(src)
    dst_pad = np.full(GROUPS * GROUP, N_NODES, np.int32)
    dst_pad[:N_EDGES] = np.asarray(dst)
    edge_pad = np.zeros((GROUPS * GROUP, F_E), np.float32)
    edge_pad[:N_EDGES] = np.asarray(edge_attr_32)
    arrays = {
        "x_t": x_pad.reshape(NODE_TILES, P, F_X).transpose(1, 0, 2).reshape(P, NODE_TILES * F_X),
        "src_t": src_pad.reshape(GROUPS * TPG, P).T,
        "dst_t": dst_pad.reshape(GROUPS * TPG, P).T,
        "edge_t": edge_pad.reshape(GROUPS, TPG, P, F_E).transpose(1, 3, 0, 2).reshape(TPG * F_E, GROUPS * P),
        "w1": L0_gnn_W1, "b1": L0_gnn_b1, "w2": L0_gnn_W2, "b2": L0_gnn_b2,
        "w3": L0_gnn_W3, "b3": L0_gnn_b3, "w4": L0_gnn_W4, "b4": L0_gnn_b4,
    }
    arrays = {f"in_{name}": np.ascontiguousarray(a) for name, a in arrays.items()}
    nc = bacc.Bacc("TRN2", target_bir_lowering=False, num_devices=1)
    args = [nc.dram_tensor(name, a.shape, mybir.dt.from_np(a.dtype), kind="ExternalInput").ap()
            for name, a in arrays.items()]
    y = nc.dram_tensor("out_y", (P, NODE_TILES * F_OUT), F32, kind="ExternalOutput").ap()
    gnn_layer(nc, *args, y)
    r = run_bass_kernel_spmd(nc, [arrays], core_ids=[0])
    y_np = np.asarray(r.results[0]["out_y"])
    return np.ascontiguousarray(y_np.reshape(P, NODE_TILES, F_OUT).transpose(1, 0, 2).reshape(NODES_PAD, F_OUT)[:N_NODES])
```

```python
from contextlib import ExitStack

import concourse.bass as bass
from concourse import mybir

F32 = mybir.dt.float32
BF16 = mybir.dt.bfloat16
I32 = mybir.dt.int32
ALU = mybir.AluOpType
ACT = mybir.ActivationFunctionType
AX = mybir.AxisListType

P = 128
N_NODES, F_X, F_E, HID, F_OUT = 12500, 64, 32, 128, 64
N_EDGES = 412500
EPS = 1e-5

TPG = 4
GROUP = TPG * P
GROUPS = -(-N_EDGES // GROUP)
BODY = 13
TURNS = GROUPS // BODY
PARTS = ((0, 7), (7, BODY))
WINDOW = 64

NODE_TILES = -(-N_NODES // P)
PAIRS = NODE_TILES // 2
PAIR = 2 * P
NODES_PAD = NODE_TILES * P
CHUNKS = 7
CPAIRS = PAIRS // CHUNKS
CTILES = 2 * CPAIRS
CCOLS = CTILES * F_X
X_BUFS = 3
PIECES = ((0, 2), (2, 4), (4, 6), (6, 7))
TURNED = ((0, 4), (4, 7))
HALVES = ((0, 8), (8, 14))

LAG = 14
EARLY_PAIRS = TURNS - LAG

assert GROUPS == TURNS * BODY and NODE_TILES == 2 * PAIRS and PAIRS == CHUNKS * CPAIRS
assert PIECES[-1][1] == TURNED[-1][1] == CPAIRS and HALVES[-1][1] == CTILES


def gnn_layer(nc, x_t, src_t, dst_t, edge_t, w1, b1, w2, b2, w3, b3, w4, b4, y_t):
    proj = nc.dram_tensor("projected_nodes", [NODES_PAD, HID], F32, kind="Internal").ap()
    proj_tiles = proj.rearrange("(i p) h -> p i h", p=P)

    ctx = ExitStack()
    with ctx:
        def sb(name, shape, dt=F32):
            return ctx.enter_context(nc.sbuf_tensor(name, shape, dt))

        def pb(name, shape):
            return ctx.enter_context(nc.psum_tensor(name, shape, F32))

        def sem(name):
            return ctx.enter_context(nc.semaphore(name))

        agg = sb("agg", [P, 2, NODES_PAD + WINDOW])
        hT = sb("hT", [P, PAIRS, P])
        dst_rel = sb("dst_rel", [P, GROUPS * TPG])
        dst_int = dst_rel[:, :].bitcast(I32)
        base_i = sb("base_i", [1, GROUPS], I32)
        base_f = sb("base_f", [1, GROUPS])
        limit = sb("limit", [1, GROUPS])
        gat = sb("gat", [P, BODY, GROUP])
        edg = sb("edg", [P, BODY, P])
        idx = sb("idx", [P, BODY * TPG], I32)
        sel = sb("sel", [P, 2, TPG, WINDOW])
        sq = sb("sq", [P, CCOLS])
        lnmean = sb("lnmean", [P, CTILES])
        lnvar = sb("lnvar", [P, CTILES])
        lnstd = sb("lnstd", [P, CTILES])
        lnrstd = sb("lnrstd", [P, 2, CTILES])
        w1x = sb("w1x", [P, 2 * HID])
        w1e = sb("w1e", [P, TPG, HID])
        w2s = sb("w2s", [P, F_OUT])
        b2row = sb("b2row", [P, F_OUT])
        w3x = sb("w3x", [P, 2, HID])
        w3a = sb("w3a", [F_OUT, HID])
        w4s = sb("w4s", [P, F_OUT])
        b1b = sb("b1b", [P, HID])
        b4b = sb("b4b", [P, F_OUT])
        b3c = sb("b3c", [P, 1])
        epsc = sb("epsc", [P, 1])
        windc = sb("windc", [P, 1])
        zero = sb("zero", [P, 1])
        spare = sb("spare", [P, 1])
        ident = sb("ident", [P, P])
        onesf = sb("onesf", [P, P])
        onesb = sb("onesb", [P, P], BF16)
        iotaf = sb("iotaf", [P, WINDOW])
        viol = sb("viol", [P, 3])
        vsum = sb("vsum", [1, 1])
        flag = sb("flag", [1, 1], I32)
        rcnt = sb("rcnt", [F_OUT, PAIR])
        mean = sb("mean", [F_OUT, PAIR])
        gact = sb("gact", [P, PAIR])
        xpair = sb("xpair", [P, 2, 2 * F_X])
        ypair = sb("ypair", [P, 2 * F_OUT])

        slots = gat[:, :, :].rearrange("p s n -> p (s n)")
        pout = slots[:, 0:2 * CTILES * HID].rearrange("p (b i h) -> p b i h", b=2, h=HID)
        xin = slots[:, 2 * CTILES * HID:2 * CTILES * HID + X_BUFS * CCOLS].rearrange("p (b n) -> p b n", b=X_BUFS)
        trash = edg[:, :, :].rearrange("p g e -> p (g e)").bitcast(BF16)[:, 0:GROUPS * TPG]
        gen_iota = slots[:, 1 * GROUP:1 * GROUP + PAIR]
        gen_sel = slots[:, 2 * GROUP:4 * GROUP].rearrange("p (j w) -> p j w", j=TPG)
        gen_dst = slots[:, 4 * GROUP:4 * GROUP + TPG]
        gen_dst_i = slots[:, 5 * GROUP:5 * GROUP + TPG].bitcast(I32)

        banks = pb("banks", [P, 8, 512])
        mps = banks[:, 0:2, :]
        wps = banks[:, 2:4, :]
        iota_ps = banks[:, 4, 0:WINDOW]
        s2_ps = banks[0:F_OUT, 5, 0:PAIR]
        g_ps = banks[:, 6, 0:PAIR]
        o_ps = banks[:, 7, 0:2 * F_OUT]
        tps = banks[:, 0:2, :].rearrange("p b (q n) -> p b q n", n=P)
        ups = [banks[:, k, :] for k in (2, 3, 5, 6)]
        base_ps = [banks[:, k, 0:GROUPS // 2] for k in (4, 7)]
        viol_ps = banks[0:1, 7, 0:3]
        gen_ps = banks[:, 2, :].rearrange("p (c n) -> p c n", c=2)

        weights_in = sem("weights_in")
        bias_in = sem("bias_in")
        dst_in = sem("dst_in")
        pad_zeroed = sem("pad_zeroed")
        pool_consts = sem("pool_consts")
        dve_consts = sem("dve_consts")
        iota_up = sem("iota_up")
        base_copied = sem("base_copied")
        base_spread = sem("base_spread")
        rel_ready = sem("rel_ready")
        limit_ready = sem("limit_ready")
        low_checked = sem("low_checked")
        all_checked = sem("all_checked")
        viol_summed = sem("viol_summed")
        vsum_ready = sem("vsum_ready")
        flag_ready = sem("flag_ready")
        x_in = [sem(f"x_in{b}") for b in range(X_BUFS)]
        ln_sum = sem("ln_sum")
        ln_mean = sem("ln_mean")
        ln_centred = sem("ln_centred")
        ln_squared = sem("ln_squared")
        ln_var = sem("ln_var")
        ln_std = sem("ln_std")
        ln_rstd = sem("ln_rstd")
        ln_scaled = sem("ln_scaled")
        ln_scaled_dve = sem("ln_scaled_dve")
        h_turned = sem("h_turned")
        h_kept = sem("h_kept")
        projected = sem("projected")
        biased = sem("biased")
        proj_out = [[sem(f"proj_out{b}{half}") for half in range(2)] for b in range(2)]
        agg_zeroed_pool = sem("agg_zeroed_pool")
        agg_zeroed_act = sem("agg_zeroed_act")
        agg_zeroed_dve = sem("agg_zeroed_dve")
        settled = sem("settled")
        idx_in = [sem(f"idx_in{h}") for h in range(2)]
        edg_in = [sem(f"edg_in{h}") for h in range(2)]
        gathered = [sem(f"gathered{s}") for s in range(BODY)]
        edge_mm = sem("edge_mm")
        summed = sem("summed")
        relued = sem("relued")
        selected = sem("selected")
        window_mm = sem("window_mm")
        accumulated = sem("accumulated")
        xpair_in = [sem(f"xpair_in{b}") for b in range(2)]
        cnt_clamped = sem("cnt_clamped")
        cnt_inverted = sem("cnt_inverted")
        w2_mm = sem("w2_mm")
        averaged = sem("averaged")
        w3_mm = sem("w3_mm")
        g_relued = sem("g_relued")
        w4_mm = sem("w4_mm")
        y_biased = sem("y_biased")
        y_ready = sem("y_ready")
        y_out = sem("y_out")
        gen_in = sem("gen_in")
        gen_gathered = sem("gen_gathered")
        gen_edge_mm = sem("gen_edge_mm")
        gen_dst_f = sem("gen_dst_f")
        gen_summed = sem("gen_summed")
        gen_relued = sem("gen_relued")
        gen_iota_up = sem("gen_iota_up")
        gen_selected = sem("gen_selected")
        gen_stepped = sem("gen_stepped")
        gen_mm = sem("gen_mm")
        gen_acc = sem("gen_acc")

        def done(i, s):
            return i * BODY + (BODY + s + 1)

        def user_before(s, bufs):
            if s >= bufs:
                return s - bufs
            return max(q for q in range(BODY) if q % bufs == s % bufs) - BODY

        def table_written(eng):
            for b in range(2):
                for half in range(2):
                    eng.wait_ge(proj_out[b][half], 16 * ((CHUNKS + 1 - b) // 2))

        agg_flat = agg[:, :, :].rearrange("p c n -> p (c n)")
        POOL_CLEARS, ACT_CLEARS, DVE_CLEARS = range(0, 6), range(6, 11), range(11, 14)
        clears = DVE_CLEARS[-1] + 1
        clear = agg_flat.shape[1] // clears

        def cleared(part):
            lo = part * clear
            return agg_flat[:, lo:lo + clear] if part < clears - 1 else agg_flat[:, lo:]

        def agg_zeroed(eng):
            eng.wait_ge(agg_zeroed_pool, len(POOL_CLEARS))
            eng.wait_ge(agg_zeroed_act, len(ACT_CLEARS))
            eng.wait_ge(agg_zeroed_dve, len(DVE_CLEARS))

        def settle(eng):
            eng.sem_inc(settled, 1)

        def path(eng, fast, general):
            eng.wait_ge(flag_ready, 1)
            taken = eng.value_load(flag[0:1, 0:1])
            with eng.If(taken == 0):
                fast()
            with eng.Else():
                general()

        block = ctx.enter_context(nc.Block())

        @block.sync
        def _(sp):
            def load_x(c):
                if c >= X_BUFS:
                    sp.wait_ge(h_turned, 2 * (c - X_BUFS) + 2)
                sp.dma_start(xin[:, c % X_BUFS, :], x_t[:, c * CCOLS:(c + 1) * CCOLS])\
                  .then_inc(x_in[c % X_BUFS], 16)

            def store_proj(c, half):
                lo, hi = HALVES[half]
                sp.wait_ge(biased, 4 * c + 2 * half + 2)
                sp.dma_start(proj_tiles[:, c * CTILES + lo:c * CTILES + hi, :], pout[:, c % 2, lo:hi, :])\
                  .then_inc(proj_out[c % 2][half], 16)

            def load_part(i, h):
                lo, hi = PARTS[h]
                sp.dma_start(idx[:, lo * TPG:hi * TPG],
                             src_t[:, bass.ds(i * (BODY * TPG) + lo * TPG, (hi - lo) * TPG)])\
                  .then_inc(idx_in[h], 16)
                sp.dma_start(edg[:, lo:hi, :].rearrange("p g e -> p (g e)"),
                             edge_t[:, bass.ds(i * (BODY * P) + lo * P, (hi - lo) * P)])\
                  .then_inc(edg_in[h], 16)

            def node_load(c, buf=0):
                sp.dma_start(xpair[:, buf, :], x_t[:, bass.ds(c * (2 * F_X), 2 * F_X)]).then_inc(xpair_in[buf], 16)

            def node_store(c):
                sp.wait_ge(y_ready, c + 1)
                sp.dma_start(y_t[:, bass.ds(c * (2 * F_OUT), 2 * F_OUT)], ypair[:, :]).then_inc(y_out, 16)
                sp.wait_ge(y_out, c * 16 + 16)
                settle(sp)

            load_x(0)
            load_x(1)
            load_x(2)
            sp.dma_start(dst_int, dst_t).then_inc(dst_in, 16)
            sp.dma_start(w2s[:, :], w2).then_inc(weights_in, 16)
            sp.dma_start(w3a[:, :], w3[F_X:F_X + F_OUT, :]).then_inc(weights_in, 16)
            sp.dma_start(w4s[:, :], w4).then_inc(weights_in, 16)
            sp.dma_start(b3c[:, :], b3.rearrange("(h a) -> h a", a=1)).then_inc(weights_in, 16)
            sp.wait_ge(pad_zeroed, 1)
            for j in range(TPG):
                sp.dma_start(w1e[j * F_E:(j + 1) * F_E, j, :], w1[F_X:F_X + F_E, :]).then_inc(weights_in, 16)
            sp.dma_start(b4b[:, :], b4.partition_broadcast(P)).then_inc(weights_in, 16)

            load_x(X_BUFS)
            for c in range(CHUNKS):
                store_proj(c, 0)
                if c + 1 + X_BUFS < CHUNKS:
                    load_x(c + 1 + X_BUFS)
                store_proj(c, 1)

            def fast():
                sp.wait_ge(all_checked, 1)
                load_part(0, 0)
                load_part(0, 1)

                def turn(i, pair):
                    for h, (lo, hi) in enumerate(PARTS):
                        if pair is not None and h == 1:
                            node_store(pair)
                        for s in range(lo, hi):
                            sp.wait_ge(gathered[s], i * (16 * TPG) + 16 * TPG)
                        settle(sp)
                        sp.wait_ge(edge_mm, done(i, hi - 1))
                        load_part(i + 1, h)
                        if pair is not None and h == 0:
                            node_load(pair)

                with sp.Fori(0, LAG) as i:
                    turn(i, None)
                with sp.Fori(0, EARLY_PAIRS - 1) as c:
                    turn(c + LAG, c)
                node_load(EARLY_PAIRS - 1)
                for c in range(EARLY_PAIRS, PAIRS):
                    node_load(c, 1)
                    node_store(c - 1)
                node_store(PAIRS - 1)

            def general():
                sp.wait_ge(all_checked, 1)
                table_written(sp)
                with sp.Fori(0, GROUPS) as k:
                    sp.wait_ge(gen_acc, (k + 1) * PAIRS)
                    sp.dma_start(idx[:, 0:TPG], src_t[:, bass.ds(k * TPG, TPG)]).then_inc(gen_in, 16)
                    sp.dma_start(gen_dst_i, dst_t[:, bass.ds(k * TPG, TPG)]).then_inc(gen_in, 16)
                    sp.dma_start(edg[:, 0, :], edge_t[:, bass.ds(k * P, P)]).then_inc(gen_in, 16)
                with sp.Fori(0, PAIRS) as c:
                    node_load(c)
                    node_store(c)

            path(sp, fast, general)

        @block.gpsimd
        def _(pool):
            pool.memset(w1e[:, :, :], 0.0).then_inc(pad_zeroed, 1)
            pool.memset(w1x[:, :], 0.0).then_inc(pad_zeroed, 1)
            pool.memset(w3x[:, :, :], 0.0).then_inc(pad_zeroed, 1)
            pool.memset(b2row[:, :], 0.0).then_inc(pad_zeroed, 1)
            pool.memset(ident[:, :], 0.0).then_inc(pool_consts, 1)
            pool.iota(iotaf[:, :], [[1, WINDOW]], base=0, channel_multiplier=0,
                      allow_small_or_imprecise_dtypes=True).then_inc(pool_consts, 1)
            pool.iota(limit[:, :], [[PAIR, TURNS], [0, BODY]], base=-PAIR * (LAG - 1), channel_multiplier=0,
                      allow_small_or_imprecise_dtypes=True).then_inc(pool_consts, 1)
            pool.wait_ge(pool_consts, 3)
            pool.affine_select(out=ident[:, :], in_=ident[:, :], compare_op=ALU.not_equal, fill=1.0, base=0,
                               pattern=[[-1, P]], channel_multiplier=1).then_inc(pool_consts, 1)

            def centre(c):
                pool.wait_ge(ln_mean, c + 1)
                v = xin[:, c % X_BUFS, :].rearrange("p (i f) -> p i f", f=F_X)
                pool.tensor_tensor(v, v, lnmean[:, :].unsqueeze(2).to_broadcast([P, CTILES, F_X]), ALU.subtract)\
                    .then_inc(ln_centred, 1)

            def scale(c, lo=0, hi=CTILES):
                pool.wait_ge(ln_rstd, c + 1)
                v = xin[:, c % X_BUFS, lo * F_X:hi * F_X].rearrange("p (i f) -> p i f", f=F_X)
                pool.tensor_tensor(v, v, lnrstd[:, c % 2, lo:hi].unsqueeze(2).to_broadcast([P, hi - lo, F_X]),
                                   ALU.mult).then_inc(ln_scaled, 1)

            def clear_agg(part):
                pool.memset(cleared(part), 0.0).then_inc(agg_zeroed_pool, 1)

            centre(0)
            centre(1)
            scale(0)
            centre(2)
            scale(1)
            for c in range(2, CHUNKS):
                clear_agg(c - 2)
                if c + 1 < CHUNKS:
                    centre(c + 1)
                if c < CHUNKS - 1:
                    scale(c)
            scale(CHUNKS - 1, 2 * TURNED[0][1])
            clear_agg(CHUNKS - 2)

            def gather(s, j, signal):
                pool.indirect_dma_start(
                    out=gat[:, s, j * P:(j + 1) * P], out_offset=None, in_=proj[:, :],
                    in_offset=bass.IndirectOffsetOnAxis(ap=idx[:, s * TPG + j:s * TPG + j + 1], axis=0))\
                    .then_inc(signal, 16)

            def fast():
                table_written(pool)
                with pool.Fori(0, TURNS) as i:
                    for s in range(BODY):
                        for h, (lo, hi) in enumerate(PARTS):
                            if s == lo:
                                pool.wait_ge(idx_in[h], i * 16 + 16)
                        pool.wait_ge(window_mm, done(i, s - BODY))
                        settle(pool)
                        for j in range(TPG):
                            gather(s, j, gathered[s])

            def general():
                table_written(pool)
                pool.iota(gen_iota, [[1, PAIR]], base=0, channel_multiplier=0,
                          allow_small_or_imprecise_dtypes=True).then_inc(gen_iota_up, 1)
                with pool.Fori(0, GROUPS) as k:
                    pool.wait_ge(gen_in, k * 48 + 48)
                    settle(pool)
                    for j in range(TPG):
                        gather(0, j, gen_gathered)

            path(pool, fast, general)

        @block.scalar
        def _(act):
            def square(c):
                act.wait_ge(ln_centred, c + 1)
                if c >= 1:
                    act.wait_ge(ln_var, c)
                nc.scalar.activation(sq[:, :], xin[:, c % X_BUFS, :], ACT.Square).then_inc(ln_squared, 1)

            def std(c):
                act.wait_ge(ln_var, c + 1)
                nc.scalar.activation(lnstd[:, :], lnvar[:, :], ACT.Sqrt, bias=epsc[:, :], scale=1.0 / F_X)\
                  .then_inc(ln_std, 1)

            def keep(c, t):
                act.wait_ge(h_turned, 2 * c + t + 1)
                lo, hi = TURNED[t]
                nc.scalar.activation(hT[:, c * CPAIRS + lo:c * CPAIRS + hi, :], tps[:, t, 0:hi - lo, :], ACT.Relu)\
                  .then_inc(h_kept, 1)

            def clear_agg(part):
                part = cleared(part)
                nc.scalar.activation(part, zero[:, :].to_broadcast([P, part.shape[1]]), ACT.Copy)\
                  .then_inc(agg_zeroed_act, 1)

            act.wait_ge(pad_zeroed, 4)
            for q in range(2):
                act.dma_start(w1x[q * F_X:(q + 1) * F_X, q * HID:(q + 1) * HID], w1[0:F_X, :])\
                   .then_inc(bias_in, 16)
            act.dma_start(b1b[:, :], b1.partition_broadcast(P)).then_inc(bias_in, 16)
            act.wait_ge(dve_consts, 4)
            nc.scalar.activation(spare[:, :], epsc[:, :], ACT.Sqrt)

            square(0)
            std(0)
            square(1)
            std(1)
            for q in range(2):
                act.dma_start(w3x[q * F_X:(q + 1) * F_X, q, :], w3[0:F_X, :]).then_inc(weights_in, 16)
            act.dma_start(b2row[0:1, :], b2.rearrange("(a n) -> a n", a=1)).then_inc(weights_in, 16)
            keep(0, 0)
            keep(0, 1)
            for c in range(CHUNKS):
                if c + 2 < CHUNKS:
                    square(c + 2)
                if c + 1 < CHUNKS:
                    keep(c + 1, 0)
                    keep(c + 1, 1)
                if c + 2 < CHUNKS:
                    std(c + 2)
                if c < 2:
                    clear_agg(ACT_CLEARS[c])
                elif c == 2:
                    act.wait_ge(rel_ready, 2)
                    nc.scalar.activation(trash, dst_rel[:, :], ACT.Relu, scale=-1.0, accum_out=viol[:, 0:1])\
                      .then_inc(low_checked, 1)
                elif c == 3:
                    act.wait_ge(low_checked, 1)
                    nc.scalar.activation(trash, dst_rel[:, :], ACT.Relu, bias=windc[:, :], accum_out=viol[:, 1:2])\
                      .then_inc(all_checked, 1)
                    act.wait_ge(limit_ready, 1)
                    nc.scalar.activation(base_f[:, :], limit[:, :], ACT.Relu, accum_out=viol[0:1, 2:3])\
                      .then_inc(all_checked, 1)
                elif c == 4:
                    clear_agg(ACT_CLEARS[2])
            clear_agg(ACT_CLEARS[3])
            clear_agg(ACT_CLEARS[4])

            def node_relu(c):
                act.wait_ge(w3_mm, c + 1)
                nc.scalar.activation(gact[:, :], g_ps, ACT.Relu, bias=b3c[:, :]).then_inc(g_relued, 1)

            act.wait_ge(weights_in, 16 * 12)

            def fast():
                def turn(i, pair):
                    for s in range(BODY):
                        act.wait_ge(summed, done(i, s))
                        nc.scalar.activation(gat[:, s, :], gat[:, s, :], ACT.Relu).then_inc(relued, 1)
                        if pair is not None and s == 5:
                            node_relu(pair)

                with act.Fori(0, LAG) as i:
                    turn(i, None)
                with act.Fori(0, EARLY_PAIRS) as c:
                    turn(c + LAG, c)
                for c in range(EARLY_PAIRS, PAIRS):
                    node_relu(c)

            def general():
                with act.Fori(0, GROUPS) as k:
                    act.wait_ge(gen_summed, k + 1)
                    nc.scalar.activation(gat[:, 0, :], gat[:, 0, :], ACT.Relu).then_inc(gen_relued, 1)
                with act.Fori(0, PAIRS) as c:
                    node_relu(c)

            path(act, fast, general)

        @block.tensor
        def _(pe):
            pe.wait_ge(pool_consts, 4)
            pe.wait_ge(bias_in, 48)

            def project(c, u):
                pe.wait_ge(h_kept, 2 * c + (1 if u < 2 else 2))
                if c >= 1:
                    pe.wait_ge(biased, 4 * (c - 1) + u + 1)
                for k, q in enumerate(range(*PIECES[u])):
                    mm = nc.tensor.matmul(ups[u][:, k * PAIR:(k + 1) * PAIR], hT[:, c * CPAIRS + q, :], w1x[:, :],
                                          start=True, stop=True)
                mm.then_inc(projected, 1)

            def turn_over(c, t):
                if c < CHUNKS - 1:
                    pe.wait_ge(ln_scaled, c + 1)
                elif t == 0:
                    pe.wait_ge(ln_scaled_dve, 1)
                else:
                    pe.wait_ge(ln_scaled, CHUNKS)
                if c >= 1:
                    pe.wait_ge(h_kept, 2 * (c - 1) + t + 1)
                lo, hi = TURNED[t]
                for q in range(lo, hi):
                    mm = nc.tensor.transpose(tps[:, t, q - lo, :], xin[:, c % X_BUFS, q * P:(q + 1) * P], ident[:, :])
                mm.then_inc(h_turned, 1)

            turn_over(0, 0)
            turn_over(0, 1)
            for c in range(CHUNKS):
                project(c, 0)
                project(c, 1)
                if c + 1 < CHUNKS:
                    turn_over(c + 1, 0)
                    turn_over(c + 1, 1)
                project(c, 2)
                project(c, 3)
                if c == 0:
                    pe.wait_ge(dve_consts, 4)
                    pe.wait_ge(base_copied, 2)
                    for h in range(2):
                        mm = nc.tensor.matmul(base_ps[h], onesf[0:1, :],
                                              base_f[0:1, h * (GROUPS // 2):(h + 1) * (GROUPS // 2)],
                                              start=True, stop=True)
                    mm.then_inc(base_spread, 1)
                if c == 4:
                    pe.wait_ge(all_checked, 2)
                    nc.tensor.matmul(viol_ps, onesf[:, 0:1], viol[:, :], start=True, stop=True)\
                      .then_inc(viol_summed, 1)

            pe.wait_ge(weights_in, 16 * 12)
            agg_zeroed(pe)
            pe.wait_ge(biased, 4 * CHUNKS)

            def edge_products(buf, s):
                return nc.tensor.matmul(mps[:, buf, :], edg[:, s, :], w1e[:, :, :].rearrange("p j h -> p (j h)"),
                                        start=True, stop=True)

            def node_w2(c):
                cols = bass.ds(c * PAIR, PAIR)
                nc.tensor.matmul(s2_ps, w2s[:, :], agg[:, 0, cols], start=True, stop=False)
                nc.tensor.matmul(s2_ps, b2row[:, :], agg[:, 1, cols], start=False, stop=True).then_inc(w2_mm, 1)

            def node_w3(c):
                pe.wait_ge(averaged, c + 1)
                nc.tensor.matmul(g_ps, w3a[:, :], mean[:, :], start=True, stop=False)
                for q in range(2):
                    mm = nc.tensor.matmul(g_ps[:, q * P:(q + 1) * P], w3x[:, q, :],
                                          hT[:, bass.ds(c, 1), :].rearrange("p a n -> p (a n)"),
                                          start=False, stop=(q == 1))
                mm.then_inc(w3_mm, 1)

            def node_w4(c):
                pe.wait_ge(g_relued, c + 1)
                for q in range(2):
                    mm = nc.tensor.matmul(o_ps[:, q * F_OUT:(q + 1) * F_OUT], gact[:, q * P:(q + 1) * P],
                                          w4s[:, :], start=True, stop=True)
                mm.then_inc(w4_mm, 1)

            def fast():
                def window_sums(i, s):
                    pe.wait_ge(relued, done(i, s))
                    pe.wait_ge(selected, done(i, s))
                    pe.wait_ge(accumulated, done(i, user_before(s, 2)))
                    for j in range(TPG):
                        nc.tensor.matmul(wps[:, s % 2, 0:WINDOW], gat[:, s, j * P:(j + 1) * P], sel[:, s % 2, j, :],
                                         start=(j == 0), stop=(j == TPG - 1))
                    for j in range(TPG):
                        mm = nc.tensor.matmul(wps[:, s % 2, WINDOW:2 * WINDOW], onesb[:, :],
                                              sel[:, s % 2, j, :].bitcast(BF16)[:, 1::2],
                                              start=(j == 0), stop=(j == TPG - 1))
                    mm.then_inc(window_mm, 1)

                def turn(i, pair):
                    for s in range(BODY):
                        for h, (lo, hi) in enumerate(PARTS):
                            if s == lo:
                                pe.wait_ge(edg_in[h], i * 16 + 16)
                        pe.wait_ge(summed, done(i, user_before(s, 2)))
                        edge_products(s % 2, s).then_inc(edge_mm, 1)
                        if s >= 1:
                            window_sums(i, s - 1)
                        if pair is not None and s == 2:
                            pe.wait_ge(accumulated, done(i, -1))
                            node_w2(pair)
                        if pair is not None and s == 4:
                            node_w3(pair)
                        if pair is not None and s == 6:
                            node_w4(pair)
                    window_sums(i, BODY - 1)

                with pe.Fori(0, LAG) as i:
                    turn(i, None)
                with pe.Fori(0, EARLY_PAIRS) as c:
                    turn(c + LAG, c)
                pe.wait_ge(accumulated, done(TURNS, -1))
                for c in range(EARLY_PAIRS, PAIRS):
                    node_w2(c)
                    node_w3(c)
                    node_w4(c)

            def general():
                with pe.Fori(0, GROUPS) as k:
                    pe.wait_ge(gen_in, k * 48 + 48)
                    edge_products(0, 0).then_inc(gen_edge_mm, 1)
                    pe.wait_ge(gen_relued, k + 1)
                    settle(pe)
                    with pe.Fori(0, PAIRS) as b:
                        pe.wait_ge(gen_selected, k * PAIRS + b + 1)
                        for j in range(TPG):
                            nc.tensor.matmul(gen_ps[:, 0, :], gat[:, 0, j * P:(j + 1) * P], gen_sel[:, j, :],
                                             start=(j == 0), stop=(j == TPG - 1))
                        for j in range(TPG):
                            mm = nc.tensor.matmul(gen_ps[:, 1, :], onesb[:, :],
                                                  gen_sel[:, j, :].bitcast(BF16)[:, 1::2],
                                                  start=(j == 0), stop=(j == TPG - 1))
                        mm.then_inc(gen_mm, 1)
                pe.wait_ge(gen_acc, (GROUPS + 1) * PAIRS)
                with pe.Fori(0, PAIRS) as c:
                    node_w2(c)
                    node_w3(c)
                    node_w4(c)

            path(pe, fast, general)

        @block.vector
        def _(dve):
            dve.sem_inc(gen_stepped, 1)
            for group_sem in (edge_mm, summed, relued, selected, window_mm, accumulated):
                dve.sem_inc(group_sem, BODY)
            dve.sem_inc(gen_acc, PAIRS)
            nc.vector.memset(onesf[:, :], 1.0).then_inc(dve_consts, 1)
            nc.vector.memset(epsc[:, :], EPS).then_inc(dve_consts, 1)
            nc.vector.memset(windc[:, :], -float(WINDOW - 1)).then_inc(dve_consts, 1)
            nc.vector.memset(onesb[:, :], 1.0)
            nc.vector.memset(zero[:, :], 0.0).then_inc(dve_consts, 1)
            nc.vector.memset(viol[:, :], 0.0).then_inc(dve_consts, 1)

            def mean_of(c):
                v = xin[:, c % X_BUFS, :].rearrange("p (i f) -> p i f", f=F_X)
                dve.wait_ge(x_in[c % X_BUFS], 16 * (c // X_BUFS) + 16)
                if c >= 1:
                    dve.wait_ge(ln_centred, c)
                nc.vector.tensor_reduce(lnmean[:, :], v, AX.X, ALU.add).then_inc(ln_sum, 1)
                dve.wait_ge(ln_sum, c + 1)
                nc.vector.tensor_scalar(lnmean[:, :], lnmean[:, :], 1.0 / F_X, None, ALU.mult).then_inc(ln_mean, 1)

            def variance(c):
                dve.wait_ge(ln_squared, c + 1)
                if c >= 1:
                    dve.wait_ge(ln_std, c)
                nc.vector.tensor_reduce(lnvar[:, :], sq[:, :].rearrange("p (i f) -> p i f", f=F_X), AX.X, ALU.add)\
                  .then_inc(ln_var, 1)

            def inverse(c):
                dve.wait_ge(ln_std, c + 1)
                if c >= 2:
                    dve.wait_ge(ln_scaled, c - 1)
                nc.vector.reciprocal(lnrstd[:, c % 2, :], lnstd[:, :]).then_inc(ln_rstd, 1)

            def bias(c, u):
                lo, hi = PIECES[u]
                dve.wait_ge(projected, 4 * c + u + 1)
                if c >= 2 and u % 2 == 0:
                    dve.wait_ge(proj_out[c % 2][u // 2], 16 * (c // 2))
                nc.vector.tensor_tensor(
                    pout[:, c % 2, 2 * lo:2 * hi, :],
                    ups[u][:, 0:(hi - lo) * PAIR].rearrange("p (i h) -> p i h", h=HID),
                    b1b[:, :].unsqueeze(1).to_broadcast([P, 2 * (hi - lo), HID]), ALU.add).then_inc(biased, 1)

            def relative(h):
                dve.wait_ge(base_spread, 1)
                half = slice(h * GROUPS * TPG // 2, (h + 1) * GROUPS * TPG // 2)
                nc.vector.tensor_tensor(
                    dst_rel[:, half].rearrange("p (g j) -> p g j", j=TPG),
                    dst_int[:, half].rearrange("p (g j) -> p g j", j=TPG),
                    base_ps[h].unsqueeze(2).to_broadcast([P, GROUPS // 2, TPG]), ALU.subtract)\
                  .then_inc(rel_ready, 1)

            mean_of(0)
            mean_of(1)
            variance(0)
            inverse(0)
            mean_of(2)
            variance(1)
            inverse(1)
            dve.wait_ge(dst_in, 16)
            first_dst = dst_int[0:1, 0:GROUPS * TPG:TPG]
            nc.vector.tensor_copy(base_f[:, :], first_dst).then_inc(base_copied, 1)
            nc.vector.tensor_copy(base_i[:, :], first_dst).then_inc(base_copied, 1)
            dve.wait_ge(bias_in, 48)

            for c in range(CHUNKS):
                bias(c, 0)
                bias(c, 1)
                if c + 2 < CHUNKS:
                    variance(c + 2)
                if c + 3 < CHUNKS:
                    mean_of(c + 3)
                if c + 2 < CHUNKS:
                    inverse(c + 2)
                if c == CHUNKS - 3:
                    hi = 2 * TURNED[0][1]
                    v = xin[:, (c + 2) % X_BUFS, 0:hi * F_X].rearrange("p (i f) -> p i f", f=F_X)
                    dve.wait_ge(ln_rstd, CHUNKS)
                    nc.vector.tensor_tensor(
                        v, v, lnrstd[:, c % 2, 0:hi].unsqueeze(2).to_broadcast([P, hi, F_X]), ALU.mult)\
                      .then_inc(ln_scaled_dve, 1)
                bias(c, 2)
                bias(c, 3)
                if c < 2:
                    relative(c)
                if c == 2:
                    dve.wait_ge(pool_consts, 3)
                    dve.wait_ge(base_copied, 1)
                    nc.vector.tensor_tensor(limit[:, :], limit[:, :], base_f[:, :], ALU.subtract)\
                      .then_inc(limit_ready, 1)
                    nc.vector.tensor_copy(iota_ps, iotaf[:, :]).then_inc(iota_up, 1)

            dve.wait_ge(viol_summed, 1)
            nc.vector.tensor_reduce(vsum[:, :], viol_ps, AX.X, ALU.add).then_inc(vsum_ready, 1)
            dve.wait_ge(vsum_ready, 1)
            nc.vector.tensor_scalar(flag[:, :], vsum[:, :], 1.0, None, ALU.min).then_inc(flag_ready, 1)

            for part in DVE_CLEARS:
                nc.vector.memset(cleared(part), 0.0).then_inc(agg_zeroed_dve, 1)
            agg_zeroed(dve)
            dve.wait_ge(iota_up, 1)

            def node_counts(c):
                nc.vector.tensor_scalar(rcnt[:, :], agg[0:F_OUT, 1, bass.ds(c * PAIR, PAIR)], 1.0, None, ALU.max)\
                  .then_inc(cnt_clamped, 1)
                dve.wait_ge(cnt_clamped, c + 1)
                nc.vector.reciprocal(rcnt[:, :], rcnt[:, :]).then_inc(cnt_inverted, 1)

            def node_mean(c):
                dve.wait_ge(w2_mm, c + 1)
                dve.wait_ge(cnt_inverted, c + 1)
                nc.vector.tensor_tensor(mean[:, :], s2_ps, rcnt[:, :], ALU.mult).then_inc(averaged, 1)

            def node_result(c, buf=0):
                dve.wait_ge(w4_mm, c + 1)
                dve.wait_ge(xpair_in[buf], (c - buf * EARLY_PAIRS) * 16 + 16)
                if buf:
                    dve.wait_ge(y_out, c * 16)
                nc.vector.tensor_tensor(ypair[:, :].rearrange("p (i f) -> p i f", f=F_OUT),
                                        o_ps.rearrange("p (i f) -> p i f", f=F_OUT),
                                        b4b[:, :].unsqueeze(1).to_broadcast([P, 2, F_OUT]), ALU.add)\
                  .then_inc(y_biased, 1)
                dve.wait_ge(y_biased, c + 1)
                nc.vector.tensor_tensor(ypair[:, :], ypair[:, :], xpair[:, buf, :], ALU.add).then_inc(y_ready, 1)

            def fast():
                def select(i, s):
                    dve.wait_ge(window_mm, done(i, user_before(s, 2)))
                    rel = dst_rel[:, bass.ds(i * (BODY * TPG) + s * TPG, TPG)]
                    nc.vector.tensor_tensor(sel[:, s % 2, :, :],
                                            iota_ps.unsqueeze(1).to_broadcast([P, TPG, WINDOW]),
                                            rel.unsqueeze(2).to_broadcast([P, TPG, WINDOW]), ALU.is_equal)\
                      .then_inc(selected, 1)

                def add_sources(i, s):
                    dve.wait_ge(edge_mm, done(i, s))
                    dve.wait_ge(gathered[s], i * (16 * TPG) + 16 * TPG)
                    nc.vector.tensor_tensor(gat[:, s, :], mps[:, s % 2, :], gat[:, s, :], ALU.add).then_inc(summed, 1)

                def accumulate(i, s):
                    base = dve.value_load(base_i[0:1, bass.ds(i * BODY + s, 1)], min_val=0, max_val=NODES_PAD)
                    dve.wait_ge(window_mm, done(i, s))
                    dve.wait_ge(accumulated, done(i, s - 1))
                    window = agg[:, :, bass.ds(base, WINDOW)]
                    nc.vector.tensor_tensor(window,
                                            wps[:, s % 2, 0:2 * WINDOW].rearrange("p (c w) -> p c w", c=2),
                                            window, ALU.add).then_inc(accumulated, 1)

                def turn(i, pair):
                    for s in range(BODY):
                        select(i, s)
                        add_sources(i, s)
                        if s >= 1:
                            accumulate(i, s - 1)
                        if pair is not None and s == 1:
                            node_counts(pair)
                        if pair is not None and s == 3:
                            node_mean(pair)
                        if pair is not None and s == 7:
                            node_result(pair)
                    accumulate(i, BODY - 1)

                with dve.Fori(0, LAG) as i:
                    turn(i, None)
                with dve.Fori(0, EARLY_PAIRS) as c:
                    turn(c + LAG, c)
                dve.wait_ge(accumulated, done(TURNS, -1))
                for c in range(EARLY_PAIRS, PAIRS):
                    node_counts(c)
                    node_mean(c)
                    node_result(c, 1)

            def general():
                dve.wait_ge(gen_iota_up, 1)
                with dve.Fori(0, GROUPS) as k:
                    dve.wait_ge(gen_in, k * 48 + 48)
                    nc.vector.tensor_copy(gen_dst, gen_dst_i).then_inc(gen_dst_f, 1)
                    dve.wait_ge(gen_edge_mm, k + 1)
                    dve.wait_ge(gen_gathered, k * (16 * TPG) + 16 * TPG)
                    nc.vector.tensor_tensor(gat[:, 0, :], mps[:, 0, :], gat[:, 0, :], ALU.add).then_inc(gen_summed, 1)
                    dve.wait_ge(gen_dst_f, k + 1)
                    settle(dve)
                    with dve.Fori(0, PAIRS) as b:
                        dve.wait_ge(gen_acc, k * PAIRS + b + PAIRS)
                        dve.wait_ge(gen_stepped, k * PAIRS + b + 1)
                        nc.vector.tensor_tensor(gen_sel, gen_iota.unsqueeze(1).to_broadcast([P, TPG, PAIR]),
                                                gen_dst.unsqueeze(2).to_broadcast([P, TPG, PAIR]), ALU.is_equal)\
                          .then_inc(gen_selected, 1)
                        dve.wait_ge(gen_mm, k * PAIRS + b + 1)
                        nc.vector.tensor_scalar(gen_dst, gen_dst, -float(PAIR), None, ALU.add).then_inc(gen_stepped, 1)
                        pair_sums = agg[:, :, bass.ds(b * PAIR, PAIR)]
                        nc.vector.tensor_tensor(pair_sums, gen_ps, pair_sums, ALU.add).then_inc(gen_acc, 1)
                dve.wait_ge(gen_acc, (GROUPS + 1) * PAIRS)
                with dve.Fori(0, PAIRS) as c:
                    node_counts(c)
                    node_mean(c)
                    node_result(c)

            path(dve, fast, general)


def kernel(x, src, dst, edge_attr_32, L0_gnn_W1, L0_gnn_b1, L0_gnn_W2, L0_gnn_b2, L0_gnn_W3, L0_gnn_b3,
           L0_gnn_W4, L0_gnn_b4):
    import numpy as np
    import concourse.bacc as bacc
    from concourse.bass_utils import run_bass_kernel_spmd

    x_pad = np.zeros((NODES_PAD, F_X), np.float32)
    x_pad[:N_NODES] = np.asarray(x)
    src_pad = np.zeros(GROUPS * GROUP, np.int32)
    src_pad[:N_EDGES] = np.asarray(src)
    dst_pad = np.full(GROUPS * GROUP, N_NODES, np.int32)
    dst_pad[:N_EDGES] = np.asarray(dst)
    edge_pad = np.zeros((GROUPS * GROUP, F_E), np.float32)
    edge_pad[:N_EDGES] = np.asarray(edge_attr_32)
    arrays = {
        "x_t": x_pad.reshape(NODE_TILES, P, F_X).transpose(1, 0, 2).reshape(P, NODE_TILES * F_X),
        "src_t": src_pad.reshape(GROUPS * TPG, P).T,
        "dst_t": dst_pad.reshape(GROUPS * TPG, P).T,
        "edge_t": edge_pad.reshape(GROUPS, TPG, P, F_E).transpose(1, 3, 0, 2).reshape(TPG * F_E, GROUPS * P),
        "w1": L0_gnn_W1, "b1": L0_gnn_b1, "w2": L0_gnn_W2, "b2": L0_gnn_b2,
        "w3": L0_gnn_W3, "b3": L0_gnn_b3, "w4": L0_gnn_W4, "b4": L0_gnn_b4,
    }
    arrays = {f"in_{name}": np.ascontiguousarray(a) for name, a in arrays.items()}
    nc = bacc.Bacc("TRN2", target_bir_lowering=False, num_devices=1)
    args = [nc.dram_tensor(name, a.shape, mybir.dt.from_np(a.dtype), kind="ExternalInput").ap()
            for name, a in arrays.items()]
    y = nc.dram_tensor("out_y", (P, NODE_TILES * F_OUT), F32, kind="ExternalOutput").ap()
    gnn_layer(nc, *args, y)
    r = run_bass_kernel_spmd(nc, [arrays], core_ids=[0])
    y_np = np.asarray(r.results[0]["out_y"])
    return np.ascontiguousarray(y_np.reshape(P, NODE_TILES, F_OUT).transpose(1, 0, 2).reshape(NODES_PAD, F_OUT)[:N_NODES])
```
